# Optimizing a Trainium2 kernel written in Bass

```python
import numpy as np
import jax
import jax.numpy as jnp

def _softmax(x, axis=-1):
    return jax.nn.softmax(x, axis=axis)

def _gelu(x):
    return jax.nn.gelu(x, approximate=True)

def _silu(x):
    return jax.nn.silu(x)

def _sigmoid(x):
    return jax.nn.sigmoid(x)

def _layernorm(x, axis=-1, eps=1e-05):
    m = jnp.mean(x, axis=axis, keepdims=True)
    v = jnp.var(x, axis=axis, keepdims=True)
    return (x - m) / jnp.sqrt(v + eps)

def _scatter_add(tgt, idx, src, axis=0):
    return tgt.at[idx].add(src)

def _segment_sum(src, seg, n):
    return jax.ops.segment_sum(src, seg, n)
kernel_name = 'mk_cond_resid_d2_seqx_r4_ea204d'

def setup_inputs(seed: int=0):
    np.random.seed(seed)
    _w = jnp.asarray

    def _rec_inputs():
        import jax
        import jax.numpy as jnp
        _rk = jax.random.key(seed)
        x = -0.000125 + 0.9999 * jax.random.normal(jax.random.fold_in(_rk, 1), (16, 256, 512), jnp.float32)
        _lenS = 256 - jax.random.randint(jax.random.fold_in(_rk, 7), (16,), 0, max(1, 256 // 4) + 1, jnp.int32)
        _lenS2 = 256 - jax.random.randint(jax.random.fold_in(_rk, 8), (16,), 0, max(1, 256 // 4) + 1, jnp.int32)
        cond_2048 = 0.000782532 + 0.100527 * jax.random.normal(jax.random.fold_in(_rk, 11), (16, 512), jnp.float32)
        return (x, cond_2048)
    x, cond_2048 = _rec_inputs()

    def _L0_cond_setup():
        import jax, jax.numpy as jnp
        import numpy as np
        key = jax.random.key(seed)
        k1, k2 = jax.random.split(key)
        B, T, C, K = (4, 1024, 512, 4)
        x = jax.random.normal(k1, (B, T, C), dtype=jnp.float32)
        w = jax.random.normal(k2, (K, 1, C), dtype=jnp.float32) * 0.1
        return {'x': x, 'w': w}
    _L0_cond_all = _L0_cond_setup()
    _L0_cond_in = {k: v for k, v in _L0_cond_all.items() if k in ()}
    del _L0_cond_all

    def _L1_cond_setup():
        import jax, jax.numpy as jnp
        import numpy as np
        B, T, D = (16, 128, 512)
        key = jax.random.key(seed)
        k0, k1, k2, k3 = jax.random.split(key, 4)
        scale = 1.0 / np.sqrt(D)
        return {'initial_state': jax.random.normal(k0, (B, D), jnp.float32), 'inputs': jax.random.normal(k1, (B, T, D), jnp.float32), 'W_ih': jax.random.normal(k2, (D, 3 * D), jnp.float32) * scale, 'W_hh': jax.random.normal(k3, (D, 3 * D), jnp.float32) * scale, 'b_ih': jnp.zeros((3 * D,), jnp.float32), 'b_hh': jnp.zeros((3 * D,), jnp.float32)}
    _L1_cond_all = _L1_cond_setup()
    _L1_cond_in = {k: v for k, v in _L1_cond_all.items() if k in ('W_ih', 'W_hh', 'b_ih', 'b_hh')}
    del _L1_cond_all
    return {'x': x, 'cond_2048': cond_2048, 'L1_cond_W_ih': _L1_cond_in['W_ih'], 'L1_cond_W_hh': _L1_cond_in['W_hh'], 'L1_cond_b_ih': _L1_cond_in['b_ih'], 'L1_cond_b_hh': _L1_cond_in['b_hh']}

def reference(x, cond_2048, L1_cond_W_ih, L1_cond_W_hh, L1_cond_b_ih, L1_cond_b_hh):
    import jax
    import jax.numpy as jnp

    def _L0_cond_ref(x, w):
        import jax, jax.numpy as jnp
        import numpy as np
        K = w.shape[0]
        C = x.shape[-1]
        y = jax.lax.conv_general_dilated(x, w, window_strides=(1,), padding=[(K - 1, 0)], dimension_numbers=('NHC', 'HIO', 'NHC'), feature_group_count=C)
        return y

    def _L1_cond_ref(initial_state, inputs, W_ih, W_hh, b_ih, b_hh):
        import jax, jax.numpy as jnp
        import numpy as np
        B, T, D = (16, 128, 512)
        "ScanOverTime(GRU cell): sequential per-timestep module call with\n            dict-state passing; merge_dict_trees stacks the per-step\n            'state_predicted' tensors along axis=1 -> [B, T, D]."

        def cell(h, x):
            gi = x @ W_ih + b_ih
            gh = h @ W_hh + b_hh
            i_r, i_z, i_n = jnp.split(gi, 3, axis=-1)
            h_r, h_z, h_n = jnp.split(gh, 3, axis=-1)
            r = jax.nn.sigmoid(i_r + h_r)
            z = jax.nn.sigmoid(i_z + h_z)
            n = jnp.tanh(i_n + r * h_n)
            h_new = (1.0 - z) * n + z * h
            return (h_new, h_new)
        xs = jnp.swapaxes(inputs, 0, 1)
        _, hs = jax.lax.scan(cell, initial_state, xs)
        return jnp.swapaxes(hs, 0, 1)
    x = x + _L0_cond_ref(x, cond_2048[:, None, :])
    x = x + _L1_cond_ref(cond_2048, x, L1_cond_W_ih, L1_cond_W_hh, L1_cond_b_ih, L1_cond_b_hh)
    return x

_drawn_inputs = setup_inputs


def setup_inputs(seed=0):
    import zlib

    import numpy as np

    out = dict(_drawn_inputs(seed))
    spreads = {'L1_cond_b_ih': (0.0, 0.1), 'L1_cond_b_hh': (0.0, 0.1)}
    factors = {}
    for name, (base, spread) in spreads.items():
        noise = np.random.default_rng([zlib.crc32(name.encode()), seed]).standard_normal(out[name].shape)
        drawn = base * np.exp(spread * noise) if base else spread * noise
        out[name] = jnp.asarray(drawn.astype(out[name].dtype))
    for name, factor in factors.items():
        out[name] = (out[name] * factor).astype(out[name].dtype)
    return out
```

```python
import concourse.bass as bass
from concourse import mybir
from contextlib import ExitStack

F32 = mybir.dt.float32
ALU = mybir.AluOpType
ACT = mybir.ActivationFunctionType

P = 128
J, C, D = 4, 4, 32
B, T, F = 16, 256, 512
K = 16
R, Z, N = 0, 1, 2
CB = C * B

BLOCKS = [4, 4, 8] + [16] * 15
STARTS = [sum(BLOCKS[:k]) for k in range(len(BLOCKS))]
NB = len(BLOCKS)
TB = max(BLOCKS)
RING = 4


def build(nc, x, cond, w_ih, w_hh, b_ih, b_hh, out):
    assert sum(BLOCKS) == T and J * D == P
    ctx = ExitStack()
    with ctx:
        def sb(name, shape):
            return ctx.enter_context(nc.sbuf_tensor(name, shape, F32))

        def pb(name):
            return ctx.enter_context(nc.psum_tensor(name, [P, 512], F32))

        def sem(name):
            return ctx.enter_context(nc.semaphore(name))

        xs = sb("xs", [P, C, (K - 1 + T) * B])
        x1 = sb("x1", [P, RING, C, TB * B])
        wih = sb("wih", [P, C, 3 * C, P])
        whh = sb("whh", [P, C, 3 * F])
        cnd = sb("cnd", [P, C, B])
        bih = sb("bih", [P, 3 * C])
        bhh = sb("bhh", [P, 3 * C])
        bsum = sb("bsum", [P, 3 * C])
        bhn = sb("bhn", [P, C, B])
        girz = sb("girz", [P, 2, 2, C, TB * B])
        gin = sb("gin", [P, 2, TB, CB, 2])
        rp = sb("rp", [P, CB, 2])
        an = sb("an", [P, CB, 2])
        zcp = sb("zcp", [P, CB, 2])
        nzh = sb("nzh", [P, CB, 2])
        hp = sb("hp", [P, 2, CB, 2])
        gt = sb("gt", [P, 3, P])
        ur = sb("ur", [P, CB])
        uz = sb("uz", [P, CB])
        zz = sb("zz", [P, CB])

        pg = pb("pg")
        pgi = [pb(f"pgi{i}") for i in range(2)]

        s_wih, s_whh, s_small, s_xl = sem("s_wih"), sem("s_whh"), sem("s_small"), [sem(f"s_xl{k}") for k in range(NB)]
        s_out = [sem(f"s_out{k}") for k in range(NB)]
        s_init = sem("s_init")
        s_bias = sem("s_bias")
        s_cv = sem("s_cv")
        s_gi = sem("s_gi")
        s_ev = sem("s_ev")
        s_gh = sem("s_gh")
        s_tr = sem("s_tr")
        s_ur = sem("s_ur")
        s_hn = sem("s_hn")
        s_uz = sem("s_uz")
        s_r = sem("s_r")
        s_zc = sem("s_zc")
        s_z = sem("s_z")
        s_zh = sem("s_zh")
        s_an = sem("s_an")
        s_n = sem("s_n")
        s_h = sem("s_h")
        s_o = sem("s_o")

        block = ctx.enter_context(nc.Block())

        def h_of(t):
            return hp[:, (t + 1) % 2, :, 1]

        step_of = [(k, t - STARTS[k]) for k in range(NB) for t in range(STARTS[k], STARTS[k] + BLOCKS[k])]
        NCV = C * K
        NU = 3 * C

        def share(total, n, i):
            return range(total * i // n, total * (i + 1) // n)

        @block.sync
        def _(sp):
            sp.dma_start(cnd[:, :, :], cond).then_inc(s_small, 16)
            sp.dma_start(bih[:, :], b_ih).then_inc(s_small, 16)
            sp.dma_start(bhh[:, :], b_hh).then_inc(s_small, 16)
            for k in range(NB):
                a, n = STARTS[k], BLOCKS[k]
                sp.dma_start(xs[:, :, (K - 1 + a) * B:(K - 1 + a + n) * B],
                             x[:, :, a * B:(a + n) * B]).then_inc(s_xl[k], 16)
            for k in range(NB):
                a, n = STARTS[k], BLOCKS[k]
                sp.wait_ge(s_o, a + n)
                sp.dma_start(out[:, :, a * B:(a + n) * B], x1[:, k % RING, :, 0:n * B]).then_inc(s_out[k], 16)
            for k in range(NB):
                sp.wait_ge(s_out[k], 16)

        @block.gpsimd
        def _(pool):
            pool.memset(xs[:, :, 0:(K - 1) * B], 0.0).then_inc(s_init, 1)
            pool.memset(rp[:, :, :], 0.0).then_inc(s_init, 1)
            pool.memset(zcp[:, :, :], 0.0).then_inc(s_init, 1)
            for t in range(T):
                k, i = step_of[t]
                pool.wait_ge(s_z, t + 1)
                if t:
                    pool.wait_ge(s_h, t + 1)
                pool.tensor_tensor(nzh[:, :, 1], zz[:, :], h_of(t - 1), ALU.mult).then_inc(s_zh, 1)
                pool.wait_ge(s_h, t + 2)
                o = x1[:, k % RING, :, i * B:(i + 1) * B]
                pool.tensor_tensor(o, o, h_of(t).rearrange("p (c b) -> p c b", c=C), ALU.add).then_inc(s_o, 1)

        @block.tensor
        def _(pe):
            def product(k, q):
                n = BLOCKS[k] * B
                u, c = divmod(q, C)
                v = NU * k + u
                if c == 0 and v >= 2:
                    pe.wait_ge(s_ev, v - 1)
                if q == 0:
                    pe.wait_ge(s_cv, NCV * (k + 1))
                m = pe.matmul(pgi[v % 2][:, 0:n], wih[:, c, u, :], x1[:, k % RING, c, 0:n],
                              start=c == 0, stop=c == C - 1)
                if c == C - 1:
                    m.then_inc(s_gi, 1)

            pe.wait_ge(s_wih, 16)
            for q in range(NU * C):
                product(0, q)
            pe.wait_ge(s_whh, 16)
            pe.wait_ge(s_bias, 9)
            for t in range(T):
                pe.wait_ge(s_h, t + 1)
                for c in range(C):
                    for j in range(J):
                        m = pe.matmul(pg[D * j:D * j + B, 0:3 * P].rearrange("p (g n) -> p g n", g=3),
                                      hp[:, t % 2, B * c:B * (c + 1), 1],
                                      whh[:, c, :].rearrange("p (g j n) -> p j g n", g=3, j=J)[:, j],
                                      start=c == 0, stop=c == C - 1)
                m.then_inc(s_gh, 1)
                k, i = step_of[t]
                if k + 1 < NB:
                    for q in share(NU * C, BLOCKS[k], i):
                        product(k + 1, q)

        @block.scalar
        def _(act):
            act.dma_start(wih[:, :, :, :], w_ih).then_inc(s_wih, 16)
            act.dma_start(whh[:, :, :], w_hh).then_inc(s_whh, 16)
            act.wait_ge(s_bias, 9)

            def copy(k, u):
                n = BLOCKS[k] * B
                v = NU * k + u
                g, c = divmod(u, C)
                act.wait_ge(s_gi, v + 1)
                if g == N:
                    o = gin[:, k % 2, 0:BLOCKS[k], c * B:(c + 1) * B, 1]
                else:
                    o = girz[:, k % 2, g, c, 0:n].rearrange("p (t b) -> p t b", b=B)
                act.activation(o, pgi[v % 2][:, 0:n].rearrange("p (t b) -> p t b", b=B), ACT.Identity, bias=bsum[:, u:u + 1]).then_inc(s_ev, 1)

            for u in range(NU):
                copy(0, u)
            for t in range(T):
                k, i = step_of[t]
                act.wait_ge(s_ur, t + 1)
                act.activation(rp[:, :, 1], ur[:, :], ACT.Sigmoid).then_inc(s_r, 1)
                act.wait_ge(s_uz, t + 1)
                act.activation(zz[:, :], uz[:, :], ACT.Sigmoid).then_inc(s_z, 1)
                act.activation(zcp[:, :, 1], uz[:, :], ACT.Sigmoid, scale=-1.0).then_inc(s_zc, 1)
                act.wait_ge(s_an, t + 1)
                act.activation(nzh[:, :, 0], an[:, :, 1], ACT.Tanh).then_inc(s_n, 1)
                if k + 1 < NB:
                    n = BLOCKS[k]
                    for u in range(NU):
                        if (u + 1) * C - 1 in share(NU * C, n, i):
                            copy(k + 1, u)

        @block.vector
        def _(dve):
            trs = [0]

            def conv(k, q):
                a, n = STARTS[k], BLOCKS[k]
                tap, c = divmod(q, C)
                if q == 0:
                    dve.wait_ge(s_xl[k], 16)
                    if k >= RING:
                        dve.wait_ge(s_out[k - RING], 16)
                if tap:
                    dve.wait_ge(s_cv, NCV * k + q - C + 1)
                o = x1[:, k % RING, c, 0:n * B]
                add = o if tap else xs[:, c, (K - 1 + a) * B:(K - 1 + a + n) * B]
                dve.scalar_tensor_tensor(o, xs[:, c, (a + tap) * B:(a + tap + n) * B], cnd[:, c, tap:tap + 1],
                                         add, ALU.mult, ALU.add).then_inc(s_cv, 1)

            def transpose(g):
                dve.transpose(gt[:, g, :], pg[:, g * P:(g + 1) * P]).then_inc(s_tr, 1)
                trs[0] += 1
                return trs[0]

            def product(g):
                return gt[:, g, :].rearrange("p (c r) -> p c r", c=C)[:, :, 0:B]

            dve.wait_ge(s_small, 48)
            dve.memset(pg[:, :], 0.0).then_inc(s_bias, 1)
            dve.tensor_tensor(bsum[:, 0:2 * C], bih[:, 0:2 * C], bhh[:, 0:2 * C], ALU.add).then_inc(s_bias, 1)
            dve.tensor_copy(bsum[:, 2 * C:], bih[:, 2 * C:]).then_inc(s_bias, 1)
            dve.memset(bhn[:, :, :], 0.0).then_inc(s_bias, 1)
            dve.wait_ge(s_bias, 4)
            for c in range(C):
                dve.tensor_scalar(bhn[:, c, :], bhn[:, c, :], bhh[:, 2 * C + c:2 * C + c + 1], None,
                                  ALU.add).then_inc(s_bias, 1)
            dve.memset(an[:, :, :], 0.0).then_inc(s_bias, 1)
            dve.wait_ge(s_init, 3)
            dve.tensor_copy(h_of(-1), cnd[:, :, :].rearrange("p c b -> p (c b)")).then_inc(s_h, 1)
            for k in range(2):
                for q in range(NCV):
                    conv(k, q)
            for t in range(T):
                k, i = step_of[t]
                todo = list(share(NCV, BLOCKS[k], i)) if k + 2 < NB else []
                early = todo[:(3 * len(todo) + 3) // 4]
                for q in early:
                    conv(k + 2, q)
                at = slice(i * B, (i + 1) * B)
                dve.wait_ge(s_gh, t + 1)
                nr = transpose(R)
                nn = transpose(N)
                nz = transpose(Z)
                if i == 0:
                    dve.wait_ge(s_ev, NU * (k + 1))
                dve.wait_ge(s_tr, nr)
                dve.tensor_tensor(ur[:, :].rearrange("p (c b) -> p c b", c=C), product(R),
                                  girz[:, k % 2, R, :, at], ALU.add).then_inc(s_ur, 1)
                dve.wait_ge(s_tr, nn)
                dve.tensor_tensor(gin[:, k % 2, i, :, 0].rearrange("p (c b) -> p c b", c=C), product(N), bhn[:, :, :],
                                  ALU.add).then_inc(s_hn, 1)
                dve.wait_ge(s_tr, nz)
                dve.tensor_tensor(uz[:, :].rearrange("p (c b) -> p c b", c=C), product(Z),
                                  girz[:, k % 2, Z, :, at], ALU.add).then_inc(s_uz, 1)
                dve.wait_ge(s_r, t + 1)
                dve.wait_ge(s_hn, t + 1)
                dve.tensor_tensor_scan(an[:, :, :].rearrange("p n s -> p (n s)"),
                                       rp[:, :, :].rearrange("p n s -> p (n s)"),
                                       gin[:, k % 2, i, :, :].rearrange("p n s -> p (n s)"),
                                       0.0, ALU.mult, ALU.add).then_inc(s_an, 1)
                for q in todo[len(early):]:
                    conv(k + 2, q)
                dve.wait_ge(s_n, t + 1)
                dve.wait_ge(s_zc, t + 1)
                dve.wait_ge(s_zh, t + 1)
                if t:
                    dve.wait_ge(s_o, t)
                dve.tensor_tensor_scan(hp[:, (t + 1) % 2, :, :].rearrange("p n s -> p (n s)"),
                                       zcp[:, :, :].rearrange("p n s -> p (n s)"),
                                       nzh[:, :, :].rearrange("p n s -> p (n s)"),
                                       0.0, ALU.mult, ALU.add).then_inc(s_h, 1)


def kernel(x, cond_2048, L1_cond_W_ih, L1_cond_W_hh, L1_cond_b_ih, L1_cond_b_hh):
    import numpy as np
    import concourse.bacc as bacc
    from concourse.bass_utils import run_bass_kernel_spmd

    def rows(a):
        return np.ascontiguousarray(np.asarray(a).reshape(J, C, D, -1).transpose(0, 2, 1, 3).reshape(P, C, -1))

    def bias(b):
        return np.ascontiguousarray(np.asarray(b).reshape(3, J, C, D).transpose(1, 3, 0, 2).reshape(P, 3 * C))

    w_ih = rows(L1_cond_W_ih).reshape(P, C, 3, J, C, D).transpose(0, 1, 2, 4, 3, 5).reshape(P, C, 3 * C, P)
    arrays = {
        "x": rows(np.asarray(x).transpose(2, 1, 0).reshape(F, T * B)),
        "cond": rows(np.asarray(cond_2048).T),
        "w_ih": np.ascontiguousarray(w_ih),
        "w_hh": rows(L1_cond_W_hh),
        "b_ih": bias(L1_cond_b_ih),
        "b_hh": bias(L1_cond_b_hh),
    }
    nc = bacc.Bacc("TRN2", target_bir_lowering=False, num_devices=1)
    args = [nc.dram_tensor(n, a.shape, F32, kind="ExternalInput").ap() for n, a in arrays.items()]
    out = nc.dram_tensor("out", (P, C, T * B), F32, kind="ExternalOutput").ap()
    build(nc, *args, out)
    r = run_bass_kernel_spmd(nc, [arrays], core_ids=[0])
    got = r.results[0]["out"].reshape(J, D, C, T, B).transpose(4, 3, 0, 2, 1)
    return np.ascontiguousarray(got.reshape(B, T, F))
```

```python
import concourse.bass as bass
from concourse import mybir
from contextlib import ExitStack

F32 = mybir.dt.float32
ALU = mybir.AluOpType
ACT = mybir.ActivationFunctionType

P = 128
J, C, D = 4, 4, 32
B, T, F = 16, 256, 512
K = 16
R, Z, N = 0, 1, 2
CB = C * B
H = 2
CH = C // H
HB = CH * B

BLOCKS = [4, 4, 8] + [16] * 15
STARTS = [sum(BLOCKS[:k]) for k in range(len(BLOCKS))]
NB = len(BLOCKS)
TB = max(BLOCKS)
RING = 4


def build(nc, x, cond, w_ih, w_hh, b_ih, b_hh, out):
    assert sum(BLOCKS) == T and J * D == P
    ctx = ExitStack()
    with ctx:
        def sb(name, shape):
            return ctx.enter_context(nc.sbuf_tensor(name, shape, F32))

        def pb(name):
            return ctx.enter_context(nc.psum_tensor(name, [P, 512], F32))

        def sem(name):
            return ctx.enter_context(nc.semaphore(name))

        xs = sb("xs", [P, C, (K - 1 + T) * B])
        x1 = sb("x1", [P, RING, C, TB * B])
        wih = sb("wih", [P, C, 3 * C, P])
        whh = sb("whh", [P, C, 3 * F])
        cnd = sb("cnd", [P, C, B])
        bih = sb("bih", [P, 3 * C])
        bhh = sb("bhh", [P, 3 * C])
        bsum = sb("bsum", [P, 3 * C])
        bhn = sb("bhn", [P, C, B])
        gi = sb("gi", [P, 2, TB, H, 2 * HB])
        gin = sb("gin", [P, 2, TB, CB, 2])
        rz = sb("rz", [P, H, 2, HB, 2])
        an = sb("an", [P, H, HB, 2])
        zcp = sb("zcp", [P, H, HB, 2])
        nzh = sb("nzh", [P, H, HB, 2])
        hp = sb("hp", [P, 2, CB, 2])
        gt = sb("gt", [P, H, 3 * CH, D])
        arg = sb("arg", [P, H, 2 * HB])

        pg = [pb(f"pg{f}") for f in range(H)]
        pgi = [pb(f"pgi{i}") for i in range(2)]

        s_wih, s_whh, s_small, s_xl = sem("s_wih"), sem("s_whh"), sem("s_small"), [sem(f"s_xl{k}") for k in range(NB)]
        s_out = [sem(f"s_out{k}") for k in range(NB)]
        s_init = sem("s_init")
        s_bias = sem("s_bias")
        s_cv = sem("s_cv")
        s_gi = sem("s_gi")
        s_ev = sem("s_ev")

        def halves(name):
            return [sem(f"{name}{f}") for f in range(H)]

        s_gh = halves("s_gh")
        s_trz = halves("s_trz")
        s_tn = halves("s_tn")
        s_u = halves("s_u")
        s_hn = halves("s_hn")
        s_rz = halves("s_rz")
        s_zc = halves("s_zc")
        s_zh = halves("s_zh")
        s_an = halves("s_an")
        s_n = halves("s_n")
        s_h = halves("s_h")
        s_o = sem("s_o")

        block = ctx.enter_context(nc.Block())

        def h_of(t, f=None):
            return hp[:, (t + 1) % 2, slice(None) if f is None else slice(f * HB, (f + 1) * HB), 1]

        def pairs(a):
            return a.rearrange("p n s -> p (n s)")

        step_of = [(k, t - STARTS[k]) for k in range(NB) for t in range(STARTS[k], STARTS[k] + BLOCKS[k])]
        NCV = C * K
        NU = 3 * C

        def share(total, n, i):
            return range(total * i // n, total * (i + 1) // n)

        @block.sync
        def _(sp):
            sp.dma_start(cnd[:, :, :], cond).then_inc(s_small, 16)
            sp.dma_start(bih[:, :], b_ih).then_inc(s_small, 16)
            sp.dma_start(bhh[:, :], b_hh).then_inc(s_small, 16)
            for k in range(NB):
                a, n = STARTS[k], BLOCKS[k]
                sp.dma_start(xs[:, :, (K - 1 + a) * B:(K - 1 + a + n) * B],
                             x[:, :, a * B:(a + n) * B]).then_inc(s_xl[k], 16)
            for k in range(NB):
                a, n = STARTS[k], BLOCKS[k]
                sp.wait_ge(s_o, a + n)
                sp.dma_start(out[:, :, a * B:(a + n) * B], x1[:, k % RING, :, 0:n * B]).then_inc(s_out[k], 16)
            for k in range(NB):
                sp.wait_ge(s_out[k], 16)

        @block.gpsimd
        def _(pool):
            pool.memset(xs[:, :, 0:(K - 1) * B], 0.0).then_inc(s_init, 1)
            pool.memset(rz[:, :, :, :, :], 0.0).then_inc(s_init, 1)
            pool.memset(zcp[:, :, :, :], 0.0).then_inc(s_init, 1)

            def add_out(t):
                k, i = step_of[t]
                for f in range(H):
                    pool.wait_ge(s_h[f], t + 2)
                o = x1[:, k % RING, :, i * B:(i + 1) * B]
                pool.tensor_tensor(o, o, h_of(t).rearrange("p (c b) -> p c b", c=C), ALU.add).then_inc(s_o, 1)

            for t in range(T):
                for f in range(H):
                    pool.wait_ge(s_rz[f], t + 1)
                    pool.wait_ge(s_h[f], t + 1)
                    pool.tensor_tensor(nzh[:, f, :, 1], rz[:, f, 1, :, 1], h_of(t - 1, f),
                                       ALU.mult).then_inc(s_zh[f], 1)
                    if f == 0 and t:
                        add_out(t - 1)
            add_out(T - 1)

        @block.tensor
        def _(pe):
            def product(k, q):
                n = BLOCKS[k] * B
                u, c = divmod(q, C)
                v = NU * k + u
                if c == 0 and v >= 2:
                    pe.wait_ge(s_ev, v - 1)
                if q == 0:
                    pe.wait_ge(s_cv, NCV * (k + 1))
                m = pe.matmul(pgi[v % 2][:, 0:n], wih[:, c, u, :], x1[:, k % RING, c, 0:n],
                              start=c == 0, stop=c == C - 1)
                if c == C - 1:
                    m.then_inc(s_gi, 1)

            pe.wait_ge(s_wih, 16)
            for q in range(NU * C):
                product(0, q)
            def recur(f, c):
                for j in range(J):
                    m = pe.matmul(pg[f][D * j:D * j + B, 0:3 * CH * D].rearrange("p (g n) -> p g n", g=3),
                                  hp[:, t % 2, B * c:B * (c + 1), 1],
                                  whh[:, c, :].rearrange("p (g j f n) -> p j f g n", g=3, j=J, f=H)[:, j, f],
                                  start=c == 0, stop=c == C - 1)
                return m

            pe.wait_ge(s_whh, 16)
            pe.wait_ge(s_bias, 10)
            for t in range(T):
                pe.wait_ge(s_h[0], t + 1)
                recur(0, 0)
                recur(0, 1)
                recur(1, 0)
                pe.wait_ge(s_h[1], t + 1)
                recur(0, 2)
                recur(0, 3).then_inc(s_gh[0], 1)
                recur(1, 1)
                recur(1, 2)
                recur(1, 3).then_inc(s_gh[1], 1)
                k, i = step_of[t]
                if k + 1 < NB:
                    for q in share(NU * C, BLOCKS[k], i):
                        product(k + 1, q)

        @block.scalar
        def _(act):
            act.dma_start(wih[:, :, :, :], w_ih).then_inc(s_wih, 16)
            act.dma_start(whh[:, :, :], w_hh).then_inc(s_whh, 16)
            act.wait_ge(s_bias, 10)

            def copy(k, u):
                n = BLOCKS[k] * B
                v = NU * k + u
                g, c = divmod(u, C)
                act.wait_ge(s_gi, v + 1)
                if g == N:
                    o = gin[:, k % 2, 0:BLOCKS[k], c * B:(c + 1) * B, 1]
                else:
                    at = (g * CH + c % CH) * B
                    o = gi[:, k % 2, 0:BLOCKS[k], c // CH, at:at + B]
                act.activation(o, pgi[v % 2][:, 0:n].rearrange("p (t b) -> p t b", b=B), ACT.Identity, bias=bsum[:, u:u + 1]).then_inc(s_ev, 1)

            for u in range(NU):
                copy(0, u)
            for t in range(T):
                k, i = step_of[t]
                for f in range(H):
                    act.wait_ge(s_u[f], t + 1)
                    act.activation(rz[:, f, :, :, 1], arg[:, f, :].rearrange("p (g n) -> p g n", g=2),
                                   ACT.Sigmoid).then_inc(s_rz[f], 1)
                    act.activation(zcp[:, f, :, 1], arg[:, f, HB:], ACT.Sigmoid, scale=-1.0).then_inc(s_zc[f], 1)
                    act.wait_ge(s_an[f], t + 1)
                    act.activation(nzh[:, f, :, 0], an[:, f, :, 1], ACT.Tanh).then_inc(s_n[f], 1)
                if k + 1 < NB:
                    n = BLOCKS[k]
                    for u in range(NU):
                        if (u + 1) * C - 1 in share(NU * C, n, i):
                            copy(k + 1, u)

        @block.vector
        def _(dve):
            def conv(k, q):
                a, n = STARTS[k], BLOCKS[k]
                tap, c = divmod(q, C)
                if q == 0:
                    dve.wait_ge(s_xl[k], 16)
                    if k >= RING:
                        dve.wait_ge(s_out[k - RING], 16)
                if tap:
                    dve.wait_ge(s_cv, NCV * k + q - C + 1)
                o = x1[:, k % RING, c, 0:n * B]
                add = o if tap else xs[:, c, (K - 1 + a) * B:(K - 1 + a + n) * B]
                dve.scalar_tensor_tensor(o, xs[:, c, (a + tap) * B:(a + tap + n) * B], cnd[:, c, tap:tap + 1],
                                         add, ALU.mult, ALU.add).then_inc(s_cv, 1)

            def transpose_rz(f):
                n = 2 * CH * D
                dve.wait_ge(s_gh[f], t + 1)
                dve.transpose(gt[:, f, 0:2 * CH, :].rearrange("p c r -> p (c r)"),
                              pg[f][:, 0:n]).then_inc(s_trz[f], 1)

            def transpose_n(f):
                n = 2 * CH * D
                dve.transpose(gt[:, f, 2 * CH:, :].rearrange("p c r -> p (c r)"),
                              pg[f][:, n:n + CH * D]).then_inc(s_tn[f], 1)

            def args_rz(f):
                dve.wait_ge(s_trz[f], t + 1)
                dve.tensor_tensor(arg[:, f, :].rearrange("p (c b) -> p c b", b=B), gt[:, f, 0:2 * CH, 0:B],
                                  gi[:, k % 2, i, f, :].rearrange("p (c b) -> p c b", b=B),
                                  ALU.add).then_inc(s_u[f], 1)

            def bias_n(f):
                dve.wait_ge(s_tn[f], t + 1)
                dve.tensor_tensor(gin[:, k % 2, i, f * HB:(f + 1) * HB, 0].rearrange("p (c b) -> p c b", c=CH),
                                  gt[:, f, 2 * CH:, 0:B], bhn[:, f * CH:(f + 1) * CH, :],
                                  ALU.add).then_inc(s_hn[f], 1)

            def scan_n(f):
                dve.wait_ge(s_hn[f], t + 1)
                dve.wait_ge(s_rz[f], t + 1)
                dve.tensor_tensor_scan(pairs(an[:, f]), pairs(rz[:, f, 0]),
                                       pairs(gin[:, k % 2, i, f * HB:(f + 1) * HB, :]),
                                       0.0, ALU.mult, ALU.add).then_inc(s_an[f], 1)

            def scan_h(f):
                dve.wait_ge(s_zc[f], t + 1)
                dve.wait_ge(s_zh[f], t + 1)
                dve.wait_ge(s_n[f], t + 1)
                if t:
                    dve.wait_ge(s_o, t - 1)
                dve.tensor_tensor_scan(pairs(hp[:, (t + 1) % 2, f * HB:(f + 1) * HB, :]),
                                       pairs(zcp[:, f]), pairs(nzh[:, f]),
                                       0.0, ALU.mult, ALU.add).then_inc(s_h[f], 1)

            dve.wait_ge(s_small, 48)
            for f in range(H):
                dve.memset(pg[f][:, :], 0.0).then_inc(s_bias, 1)
            dve.tensor_tensor(bsum[:, 0:2 * C], bih[:, 0:2 * C], bhh[:, 0:2 * C], ALU.add).then_inc(s_bias, 1)
            dve.tensor_copy(bsum[:, 2 * C:], bih[:, 2 * C:]).then_inc(s_bias, 1)
            dve.memset(bhn[:, :, :], 0.0).then_inc(s_bias, 1)
            dve.wait_ge(s_bias, 5)
            for c in range(C):
                dve.tensor_scalar(bhn[:, c, :], bhn[:, c, :], bhh[:, 2 * C + c:2 * C + c + 1], None,
                                  ALU.add).then_inc(s_bias, 1)
            dve.memset(an[:, :, :, :], 0.0).then_inc(s_bias, 1)
            dve.wait_ge(s_init, 3)
            for f in range(H):
                dve.tensor_copy(h_of(-1, f).rearrange("p (c b) -> p c b", c=CH),
                                cnd[:, f * CH:(f + 1) * CH, :]).then_inc(s_h[f], 1)
            for k in range(2):
                for q in range(NCV):
                    conv(k, q)
            for t in range(T):
                k, i = step_of[t]
                todo = list(share(NCV, BLOCKS[k], i)) if k + 2 < NB else []
                todo.reverse()

                def fill(n):
                    for _ in range(min(n, len(todo))):
                        conv(k + 2, todo.pop())

                if i == 0:
                    dve.wait_ge(s_ev, NU * (k + 1))
                transpose_rz(0)
                transpose_n(0)
                args_rz(0)
                bias_n(0)
                fill(1)
                scan_n(0)
                transpose_rz(1)
                transpose_n(1)
                args_rz(1)
                scan_h(0)
                bias_n(1)
                scan_n(1)
                fill(1)
                scan_h(1)
                fill(len(todo))


def kernel(x, cond_2048, L1_cond_W_ih, L1_cond_W_hh, L1_cond_b_ih, L1_cond_b_hh):
    import numpy as np
    import concourse.bacc as bacc
    from concourse.bass_utils import run_bass_kernel_spmd

    def rows(a):
        return np.ascontiguousarray(np.asarray(a).reshape(J, C, D, -1).transpose(0, 2, 1, 3).reshape(P, C, -1))

    def bias(b):
        return np.ascontiguousarray(np.asarray(b).reshape(3, J, C, D).transpose(1, 3, 0, 2).reshape(P, 3 * C))

    w_ih = rows(L1_cond_W_ih).reshape(P, C, 3, J, C, D).transpose(0, 1, 2, 4, 3, 5).reshape(P, C, 3 * C, P)
    arrays = {
        "x": rows(np.asarray(x).transpose(2, 1, 0).reshape(F, T * B)),
        "cond": rows(np.asarray(cond_2048).T),
        "w_ih": np.ascontiguousarray(w_ih),
        "w_hh": rows(L1_cond_W_hh),
        "b_ih": bias(L1_cond_b_ih),
        "b_hh": bias(L1_cond_b_hh),
    }
    nc = bacc.Bacc("TRN2", target_bir_lowering=False, num_devices=1)
    args = [nc.dram_tensor(n, a.shape, F32, kind="ExternalInput").ap() for n, a in arrays.items()]
    out = nc.dram_tensor("out", (P, C, T * B), F32, kind="ExternalOutput").ap()
    build(nc, *args, out)
    r = run_bass_kernel_spmd(nc, [arrays], core_ids=[0])
    got = r.results[0]["out"].reshape(J, D, C, T, B).transpose(4, 3, 0, 2, 1)
    return np.ascontiguousarray(got.reshape(B, T, F))
```

```python
import concourse.bass as bass
from concourse import mybir
from contextlib import ExitStack

F32 = mybir.dt.float32
F32R = mybir.dt.float32r
ALU = mybir.AluOpType
ACT = mybir.ActivationFunctionType

P = 128
J, C, D = 4, 4, 32
B, T, F = 16, 256, 512
K = 16
R, Z, N = 0, 1, 2
CB = C * B
H = 2
CH = C // H
HB = CH * B

BLOCKS = [8, 8] + [16] * 15
STARTS = [sum(BLOCKS[:k]) for k in range(len(BLOCKS))]
NB = len(BLOCKS)
TB = max(BLOCKS)
LAP = 128
WARM = 60
WHOLE = 2
FIRST = 2
HELPED = 3
PROD = 4
AHEAD = 5
RING = 4


def build(nc, x, cond, w_ih, w_hh, b_ih, b_hh, out):
    assert sum(BLOCKS) == T and J * D == P
    ctx = ExitStack()
    with ctx:
        def sb(name, shape, dt=F32):
            return ctx.enter_context(nc.sbuf_tensor(name, shape, dt))

        def pb(name):
            return ctx.enter_context(nc.psum_tensor(name, [P, 512], F32))

        def sem(name):
            return ctx.enter_context(nc.semaphore(name))

        xs = sb("xs", [P, C, (K - 1 + LAP) * B])
        x1 = sb("x1", [P, RING, C, TB * B])
        xhi, xlo = (sb(n, [P, 2, C, TB * B], F32R) for n in ("xhi", "xlo"))
        whi, wlo = (sb(n, [P, C, 3 * C * P], F32R) for n in ("whi", "wlo"))
        wih = sb("wih", [P, C, 3 * C * P])
        whh = sb("whh", [P, C, 3 * F])
        prod = sb("prod", [P, PROD, TB * B])
        cnd = sb("cnd", [P, C, B])
        bih = sb("bih", [P, 3 * C])
        bhh = sb("bhh", [P, 3 * C])
        bsum = sb("bsum", [P, 3 * C])
        bhn = sb("bhn", [P, C, B])
        gates = sb("gates", [P, 2, TB, 4 * CB])
        rz = sb("rz", [P, H, 2, HB, 2])
        an = sb("an", [P, H, HB, 2])
        zcp = sb("zcp", [P, H, HB, 2])
        nzh = sb("nzh", [P, H, HB, 2])
        hp = sb("hp", [P, 2, CB, 2])
        gt = sb("gt", [P, H, 3 * CH, D])
        arg = sb("arg", [P, H, 2 * HB])
        zeros = sb("zeros", [P, 512], mybir.dt.bfloat16)

        pg = [pb(f"pg{f}") for f in range(H)]
        pgi = [pb(f"pgi{i}") for i in range(2)]
        pwarm = pb("pwarm")

        s_wih = [sem(f"s_wih{c}") for c in range(C)]
        s_whh = sem("s_whh")
        s_small = sem("s_small")
        s_xl = [sem(f"s_xl{k}") for k in range(NB)]
        s_out = [sem(f"s_out{k}") for k in range(NB)]
        s_init = sem("s_init")
        s_bias = sem("s_bias")
        s_cv = sem("s_cv")
        s_pr = sem("s_pr")
        s_pa = sem("s_pa")
        s_xhi = sem("s_xhi")
        s_xlo = sem("s_xlo")
        s_whi = sem("s_whi")
        s_wlo = sem("s_wlo")
        s_gi = sem("s_gi")
        s_ev = sem("s_ev")

        def halves(name):
            return [sem(f"{name}{f}") for f in range(H)]

        s_gh = halves("s_gh")
        s_trz = halves("s_trz")
        s_tn = halves("s_tn")
        s_u = halves("s_u")
        s_hn = halves("s_hn")
        s_rz = halves("s_rz")
        s_zc = halves("s_zc")
        s_zh = halves("s_zh")
        s_an = halves("s_an")
        s_n = halves("s_n")
        s_h = halves("s_h")
        s_o = sem("s_o")

        block = ctx.enter_context(nc.Block())

        def h_of(t, f=None):
            return hp[:, (t + 1) % 2, slice(None) if f is None else slice(f * HB, (f + 1) * HB), 1]

        def gi(k, i, f):
            return gates[:, k % 2, i, f * 2 * HB:(f + 1) * 2 * HB]

        def gin(k, i, a, n):
            at = 2 * CB + 2 * a
            if isinstance(i, slice):
                return gates[:, k % 2, i, at:at + 2 * n].rearrange("p t (n s) -> p t n s", s=2)
            return gates[:, k % 2, i, at:at + 2 * n].rearrange("p (n s) -> p n s", s=2)

        def pairs(a):
            return a.rearrange("p n s -> p (n s)")

        step_of = [(k, t - STARTS[k]) for k in range(NB) for t in range(STARTS[k], STARTS[k] + BLOCKS[k])]

        def conv_ops(k):
            if k < HELPED:
                return [(tap, c) for tap in range(K) for c in range(C - 1)]
            return [(tap, c) for two in (0, 2) for tap in range(K) for c in (two, two + 1)]

        CONVOLVED = [sum(len(conv_ops(m)) for m in range(k + 1)) for k in range(NB)]
        NU = 3 * C

        def share(total, window, t):
            a, b = window
            return range(total * min(max(t - a, 0), b - a) // (b - a), total * min(max(t + 1 - a, 0), b - a) // (b - a))

        CONV = {2: (0, 7), 3: (7, 15)} | {k: (STARTS[k] - 2 * TB, STARTS[k] - TB - 2) for k in range(4, NB)}
        SPLIT = {2: (7, 7, 7, 7), 3: (11, 12, 15, 15)}
        SPLIT |= {k: tuple(STARTS[k] - TB + d for d in (-8, -7, -2, -1)) for k in range(4, NB)}
        PRODUCT = {1: (0, STARTS[1]), 2: (8, STARTS[2])} | {k: (STARTS[k] - TB, STARTS[k]) for k in range(3, NB)}

        def parts(k):
            return 1 if k < WHOLE else 3

        def units_done(k, t):
            per = C * parts(k)
            return [q // per for q in share(NU * per, PRODUCT[k], t) if q % per == per - 1]

        @block.sync
        def _(sp):
            def store(k):
                a, n = STARTS[k], BLOCKS[k]
                sp.wait_ge(s_o, a + n)
                sp.dma_start(out[:, :, a * B:(a + n) * B], x1[:, k % RING, :, 0:n * B]).then_inc(s_out[k], 16)

            sp.dma_start(cnd[:, :, :], cond).then_inc(s_small, 16)
            sp.dma_start(bih[:, :], b_ih).then_inc(s_small, 16)
            sp.dma_start(bhh[:, :], b_hh).then_inc(s_small, 16)
            for k in range(NB):
                a, n = STARTS[k], BLOCKS[k]
                if k == 2:
                    sp.wait_ge(s_whh, 16)
                if a >= LAP:
                    sp.wait_ge(s_cv, CONVOLVED[STARTS.index(a - LAP + n)])
                before = K - 1 if a == LAP else 0
                at = K - 1 + a % LAP
                sp.dma_start(xs[:, :, (at - before) * B:(at + n) * B],
                             x[:, :, (a - before) * B:(a + n) * B]).then_inc(s_xl[k], 16)
                if k >= AHEAD:
                    store(k - AHEAD)
            for k in range(NB - AHEAD, NB):
                store(k)
            for k in range(NB):
                sp.wait_ge(s_out[k], 16)

        @block.gpsimd
        def _(pool):
            pool.memset(zeros[:, :], 0.0).then_inc(s_init, 1)
            pool.memset(xs[:, :, 0:(K - 1) * B], 0.0).then_inc(s_init, 1)
            pool.memset(rz[:, :, :, :, :], 0.0).then_inc(s_init, 1)
            pool.memset(zcp[:, :, :, :], 0.0).then_inc(s_init, 1)

            def xlo_of(k, c):
                pool.wait_ge(s_xhi, C * (k - WHOLE) + c + 1)
                n = BLOCKS[k] * B
                pool.tensor_tensor(xlo[:, k % 2, c, 0:n], x1[:, k % RING, c, 0:n],
                                   xhi[:, k % 2, c, 0:n].bitcast(F32), ALU.subtract).then_inc(s_xlo, 1)

            def wlo_of(q):
                c, at = q // 2, slice(q % 2 * 3 * F // 2, (q % 2 + 1) * 3 * F // 2)
                pool.wait_ge(s_whi, c + 1)
                pool.tensor_tensor(wlo[:, c, at], wih[:, c, at], whi[:, c, at].bitcast(F32),
                                   ALU.subtract).then_inc(s_wlo, 1)

            def add_tap(k, tap):
                v, a, n = K * k + tap, STARTS[k], BLOCKS[k]
                o = x1[:, k % RING, C - 1, 0:n * B]
                pool.wait_ge(s_pr, v + 1)
                if tap:
                    pool.wait_ge(s_pa, v)
                else:
                    pool.wait_ge(s_xl[k], 16)
                pool.tensor_tensor(o, o if tap else xs[:, C - 1, (K - 1 + a) * B:(K - 1 + a + n) * B],
                                   prod[:, v % PROD, 0:n * B], ALU.add).then_inc(s_pa, 1)

            for tap in range(K):
                add_tap(0, tap)
            wlo_of(0)
            wlo_of(1)
            for tap in range(K):
                add_tap(1, tap)

            def add_out(t):
                k, i = step_of[t]
                for f in range(H):
                    pool.wait_ge(s_h[f], t + 2)
                o = x1[:, k % RING, :, i * B:(i + 1) * B]
                pool.tensor_tensor(o, o, h_of(t).rearrange("p (c b) -> p c b", c=C), ALU.add).then_inc(s_o, 1)

            for t in range(T):
                for f in range(H):
                    pool.wait_ge(s_rz[f], t + 1)
                    pool.wait_ge(s_h[f], t + 1)
                    pool.tensor_tensor(nzh[:, f, :, 1], rz[:, f, 1, :, 1], h_of(t - 1, f),
                                       ALU.mult).then_inc(s_zh[f], 1)
                    if f == 0 and t:
                        add_out(t - 1)
                if t < 2 * C - 2:
                    wlo_of(2 + t)
                for m in range(FIRST, HELPED):
                    for tap in share(K, CONV[m], t):
                        add_tap(m, tap)
                for m, steps in SPLIT.items():
                    for c in range(C):
                        if t == steps[c]:
                            xlo_of(m, c)
            add_out(T - 1)

        @block.tensor
        def _(pe):
            def product(k, q):
                n = BLOCKS[k] * B
                m = parts(k)
                u, c, part = q // (m * C), q // m % C, q % m
                v = NU * k + u
                if c == part == 0 and v >= 2:
                    pe.wait_ge(s_ev, v - 1)
                o = pgi[v % 2][:, 0:n]
                flags = {"start": c == part == 0, "stop": c == C - 1 and part == m - 1}
                if k < WHOLE:
                    if q == 0:
                        pe.wait_ge(s_cv, CONVOLVED[k])
                        pe.wait_ge(s_pa, K * (k + 1))
                    ins = pe.matmul(o, wih[:, c, u * P:(u + 1) * P], x1[:, k % RING, c, 0:n], **flags)
                else:
                    if q == 0:
                        pe.wait_ge(s_xlo, C * (k - WHOLE + 1))
                        pe.wait_ge(s_wlo, 2 * C)
                    w, xx = ((wlo, xhi), (whi, xlo), (whi, xhi))[part]
                    ins = pe.matmul(o, w[:, c, u * P:(u + 1) * P], xx[:, k % 2, c, 0:n], **flags)
                if flags["stop"]:
                    ins.then_inc(s_gi, 1)

            pe.wait_ge(s_init, 1)
            for _ in range(WARM):
                pe.matmul(pwarm[:, :], zeros[:, 0:P], zeros[:, :], start=True, stop=True)
            for c in range(C):
                pe.wait_ge(s_wih[c], 16)
            for q in range(NU * C):
                product(0, q)

            def recur(f, c):
                for j in range(J):
                    m = pe.matmul(pg[f][D * j:D * j + B, 0:3 * CH * D].rearrange("p (g n) -> p g n", g=3),
                                  hp[:, t % 2, B * c:B * (c + 1), 1],
                                  whh[:, c, :].rearrange("p (g j f n) -> p j f g n", g=3, j=J, f=H)[:, j, f],
                                  start=c == 0, stop=c == C - 1)
                return m

            pe.wait_ge(s_whh, 16)
            pe.wait_ge(s_bias, 10)
            for t in range(T):
                pe.wait_ge(s_h[0], t + 1)
                recur(0, 0)
                recur(0, 1)
                recur(1, 0)
                pe.wait_ge(s_h[1], t + 1)
                recur(0, 2)
                recur(0, 3).then_inc(s_gh[0], 1)
                recur(1, 1)
                recur(1, 2)
                recur(1, 3).then_inc(s_gh[1], 1)
                k, _ = step_of[t]
                if k + 1 < NB:
                    for q in share(NU * C * parts(k + 1), PRODUCT[k + 1], t):
                        product(k + 1, q)

        @block.scalar
        def _(act):
            act.wait_ge(s_xl[0], 16)
            for c in range(C):
                act.dma_start(wih[:, c, :], w_ih[:, c, :]).then_inc(s_wih[c], 16)
            act.dma_start(whh[:, :, :], w_hh).then_inc(s_whh, 16)

            def xhi_of(k, c):
                if k < HELPED and c == C - 1:
                    act.wait_ge(s_pa, K * (k + 1))
                else:
                    act.wait_ge(s_cv, CONVOLVED[k - 1] + conv_ops(k).index((K - 1, c)) + 1)
                if k >= WHOLE + 2:
                    act.wait_ge(s_gi, NU * (k - 1))
                n = BLOCKS[k] * B
                act.activation(xhi[:, k % 2, c, 0:n], x1[:, k % RING, c, 0:n], ACT.Copy).then_inc(s_xhi, 1)

            def whi_of(c):
                act.wait_ge(s_wih[c], 16)
                act.activation(whi[:, c, :], wih[:, c, :], ACT.Copy).then_inc(s_whi, 1)

            def tap_product(k, tap):
                v, a, n = K * k + tap, STARTS[k], BLOCKS[k]
                act.wait_ge(s_xl[k], 16)
                if v >= PROD:
                    act.wait_ge(s_pa, v - PROD + 1)
                act.activation(prod[:, v % PROD, 0:n * B], xs[:, C - 1, (a + tap) * B:(a + tap + n) * B], ACT.Copy,
                               scale=cnd[:, C - 1, tap:tap + 1]).then_inc(s_pr, 1)

            def copy(k, u):
                n = BLOCKS[k] * B
                v = NU * k + u
                g, c = divmod(u, C)
                act.wait_ge(s_gi, v + 1)
                if g == N:
                    o = gin(k, slice(0, BLOCKS[k]), c * B, B)[:, :, :, 1]
                else:
                    o = gi(k, slice(0, BLOCKS[k]), c // CH)[:, :, (g * CH + c % CH) * B:(g * CH + c % CH + 1) * B]
                act.activation(o, pgi[v % 2][:, 0:n].rearrange("p (t b) -> p t b", b=B), ACT.Identity,
                               bias=bsum[:, u:u + 1]).then_inc(s_ev, 1)

            act.wait_ge(s_small, 48)
            act.wait_ge(s_init, 4)
            for tap in range(K):
                tap_product(0, tap)
            whi_of(0)
            whi_of(1)
            act.wait_ge(s_bias, 10)
            for u in range(NU):
                for tap in range(K * u // NU, K * (u + 1) // NU):
                    tap_product(1, tap)
                copy(0, u)
            whi_of(2)
            whi_of(3)
            for t in range(T):
                k, i = step_of[t]
                for f in range(H):
                    act.wait_ge(s_u[f], t + 1)
                    act.activation(rz[:, f, :, :, 1], arg[:, f, :].rearrange("p (g n) -> p g n", g=2),
                                   ACT.Sigmoid).then_inc(s_rz[f], 1)
                    act.activation(zcp[:, f, :, 1], arg[:, f, HB:], ACT.Sigmoid, scale=-1.0).then_inc(s_zc[f], 1)
                    act.wait_ge(s_an[f], t + 1)
                    act.activation(nzh[:, f, :, 0], an[:, f, :, 1], ACT.Tanh).then_inc(s_n[f], 1)
                for m in range(FIRST, HELPED):
                    for tap in share(K, CONV[m], t):
                        tap_product(m, tap)
                for m, steps in SPLIT.items():
                    for c in range(C):
                        if t == steps[c]:
                            xhi_of(m, c)
                if k + 1 < NB:
                    for u in units_done(k + 1, t):
                        copy(k + 1, u)

        @block.vector
        def _(dve):
            def conv(k, q):
                a, n = STARTS[k] % LAP, BLOCKS[k]
                ops = conv_ops(k)
                tap, c = ops[q]
                if q == 0:
                    dve.wait_ge(s_xl[k], 16)
                    if k >= RING:
                        dve.wait_ge(s_out[k - RING], 16)
                if tap:
                    dve.wait_ge(s_cv, CONVOLVED[k] - len(ops) + ops.index((tap - 1, c)) + 1)
                o = x1[:, k % RING, c, 0:n * B]
                add = o if tap else xs[:, c, (K - 1 + a) * B:(K - 1 + a + n) * B]
                dve.scalar_tensor_tensor(o, xs[:, c, (a + tap) * B:(a + tap + n) * B], cnd[:, c, tap:tap + 1],
                                         add, ALU.mult, ALU.add).then_inc(s_cv, 1)

            def transpose_rz(f):
                n = 2 * CH * D
                dve.wait_ge(s_gh[f], t + 1)
                dve.transpose(gt[:, f, 0:2 * CH, :].rearrange("p c r -> p (c r)"),
                              pg[f][:, 0:n]).then_inc(s_trz[f], 1)

            def transpose_n(f):
                n = 2 * CH * D
                dve.transpose(gt[:, f, 2 * CH:, :].rearrange("p c r -> p (c r)"),
                              pg[f][:, n:n + CH * D]).then_inc(s_tn[f], 1)

            def args_rz(f):
                dve.wait_ge(s_trz[f], t + 1)
                dve.tensor_tensor(arg[:, f, :].rearrange("p (c b) -> p c b", b=B), gt[:, f, 0:2 * CH, 0:B],
                                  gi(k, i, f).rearrange("p (c b) -> p c b", b=B),
                                  ALU.add).then_inc(s_u[f], 1)

            def bias_n(f):
                dve.wait_ge(s_tn[f], t + 1)
                dve.tensor_tensor(gin(k, i, f * HB, HB)[:, :, 0].rearrange("p (c b) -> p c b", c=CH),
                                  gt[:, f, 2 * CH:, 0:B], bhn[:, f * CH:(f + 1) * CH, :],
                                  ALU.add).then_inc(s_hn[f], 1)

            def scan_n(f):
                dve.wait_ge(s_hn[f], t + 1)
                dve.wait_ge(s_rz[f], t + 1)
                dve.tensor_tensor_scan(pairs(an[:, f]), pairs(rz[:, f, 0]),
                                       pairs(gin(k, i, f * HB, HB)),
                                       0.0, ALU.mult, ALU.add).then_inc(s_an[f], 1)

            def scan_h(f):
                dve.wait_ge(s_zc[f], t + 1)
                dve.wait_ge(s_zh[f], t + 1)
                dve.wait_ge(s_n[f], t + 1)
                if t > 1:
                    dve.wait_ge(s_o, t - 1)
                dve.tensor_tensor_scan(pairs(hp[:, (t + 1) % 2, f * HB:(f + 1) * HB, :]),
                                       pairs(zcp[:, f]), pairs(nzh[:, f]),
                                       0.0, ALU.mult, ALU.add).then_inc(s_h[f], 1)

            for f in range(H):
                dve.memset(pg[f][:, :], 0.0).then_inc(s_bias, 1)
            dve.memset(an[:, :, :, :], 0.0).then_inc(s_bias, 1)
            dve.memset(bhn[:, :, :], 0.0).then_inc(s_bias, 1)
            dve.wait_ge(s_small, 48)
            dve.wait_ge(s_init, 4)
            for q in range(len(conv_ops(0))):
                conv(0, q)
            dve.tensor_tensor(bsum[:, 0:2 * C], bih[:, 0:2 * C], bhh[:, 0:2 * C], ALU.add).then_inc(s_bias, 1)
            dve.tensor_copy(bsum[:, 2 * C:], bih[:, 2 * C:]).then_inc(s_bias, 1)
            dve.wait_ge(s_bias, 4)
            for c in range(C):
                dve.tensor_scalar(bhn[:, c, :], bhn[:, c, :], bhh[:, 2 * C + c:2 * C + c + 1], None,
                                  ALU.add).then_inc(s_bias, 1)
            for f in range(H):
                dve.tensor_copy(h_of(-1, f).rearrange("p (c b) -> p c b", c=CH),
                                cnd[:, f * CH:(f + 1) * CH, :]).then_inc(s_h[f], 1)
            for q in range(len(conv_ops(1))):
                conv(1, q)
            for t in range(T):
                k, i = step_of[t]
                todo = [(m, q) for m in CONV for q in share(len(conv_ops(m)), CONV[m], t)]
                todo.reverse()

                def fill(n):
                    for _ in range(min(n, len(todo))):
                        conv(*todo.pop())

                if i == 0:
                    dve.wait_ge(s_ev, NU * (k + 1))
                transpose_rz(0)
                transpose_n(0)
                args_rz(0)
                bias_n(0)
                fill(1)
                scan_n(0)
                transpose_rz(1)
                transpose_n(1)
                args_rz(1)
                scan_h(0)
                bias_n(1)
                scan_n(1)
                fill(1)
                scan_h(1)
                fill(len(todo))
    return nc


def kernel(x, cond_2048, L1_cond_W_ih, L1_cond_W_hh, L1_cond_b_ih, L1_cond_b_hh):
    import numpy as np
    import concourse.bacc as bacc
    from concourse.bass_utils import run_bass_kernel_spmd

    def rows(a):
        return np.ascontiguousarray(np.asarray(a).reshape(J, C, D, -1).transpose(0, 2, 1, 3).reshape(P, C, -1))

    def bias(b):
        return np.ascontiguousarray(np.asarray(b).reshape(3, J, C, D).transpose(1, 3, 0, 2).reshape(P, 3 * C))

    w_ih = rows(L1_cond_W_ih).reshape(P, C, 3, J, C, D).transpose(0, 1, 2, 4, 3, 5).reshape(P, C, 3 * C, P)
    arrays = {
        "x": rows(np.asarray(x).transpose(2, 1, 0).reshape(F, T * B)),
        "cond": rows(np.asarray(cond_2048).T),
        "w_ih": np.ascontiguousarray(w_ih),
        "w_hh": rows(L1_cond_W_hh),
        "b_ih": bias(L1_cond_b_ih),
        "b_hh": bias(L1_cond_b_hh),
    }
    nc = bacc.Bacc("TRN2", target_bir_lowering=False, num_devices=1)
    args = [nc.dram_tensor(n, a.shape, F32, kind="ExternalInput").ap() for n, a in arrays.items()]
    out = nc.dram_tensor("out", (P, C, T * B), F32, kind="ExternalOutput").ap()
    build(nc, *args, out)
    r = run_bass_kernel_spmd(nc, [arrays], core_ids=[0])
    got = r.results[0]["out"].reshape(J, D, C, T, B).transpose(4, 3, 0, 2, 1)
    return np.ascontiguousarray(got.reshape(B, T, F))
```
